# Optimizing a Trainium2 kernel written in Bass

```python
import numpy as np
import jax
import jax.numpy as jnp

def _softmax(x, axis=-1):
    return jax.nn.softmax(x, axis=axis)

def _gelu(x):
    return jax.nn.gelu(x, approximate=True)

def _silu(x):
    return jax.nn.silu(x)

def _sigmoid(x):
    return jax.nn.sigmoid(x)

def _layernorm(x, axis=-1, eps=1e-05):
    m = jnp.mean(x, axis=axis, keepdims=True)
    v = jnp.var(x, axis=axis, keepdims=True)
    return (x - m) / jnp.sqrt(v + eps)

def _scatter_add(tgt, idx, src, axis=0):
    return tgt.at[idx].add(src)

def _segment_sum(src, seg, n):
    return jax.ops.segment_sum(src, seg, n)
kernel_name = 'mk_rec_standalone_d1_rec_r8_f21417'

def setup_inputs(seed: int=0):
    np.random.seed(seed)
    _w = jnp.asarray

    def _rec_inputs():
        import jax
        import jax.numpy as jnp
        _rk = jax.random.key(seed)
        r_user_item_matrix = jax.random.uniform(jax.random.fold_in(_rk, 1), (2048, 750), jnp.float32, 0.0, 1)
        r_user_emb = -2.51807e-05 + 0.0199885 * jax.random.normal(jax.random.fold_in(_rk, 2), (2048, 64), jnp.float32)
        return (r_user_item_matrix, r_user_emb)
    r_user_item_matrix, r_user_emb = _rec_inputs()

    def _L0_rec_setup():
        import jax, jax.numpy as jnp
        import numpy as np
        U, I, F, H = (1000, 750, 128, 64)
        key = jax.random.key(seed)
        ks = jax.random.split(key, 7)
        return {'user_item_matrix': jax.random.uniform(ks[0], (U, I), dtype=jnp.float32), 'item_feature_matrix': jax.random.normal(ks[1], (I, F), dtype=jnp.float32), 'user_emb': jax.random.normal(ks[2], (U, H), dtype=jnp.float32) * 0.02, 'feat_w': jax.random.normal(ks[3], (F, H), dtype=jnp.float32) * (1.0 / np.sqrt(F)), 'feat_b': jax.random.normal(ks[4], (H,), dtype=jnp.float32) * 0.01, 'gcn_w': jax.random.normal(ks[5], (H, H), dtype=jnp.float32) * (1.0 / np.sqrt(H)), 'gcn_b': jax.random.normal(ks[6], (H,), dtype=jnp.float32) * 0.01}
    _L0_rec_all = _L0_rec_setup()
    _L0_rec_in = {k: v for k, v in _L0_rec_all.items() if k in ('item_feature_matrix', 'feat_w', 'feat_b', 'gcn_w', 'gcn_b')}
    del _L0_rec_all
    return {'r_user_item_matrix': r_user_item_matrix, 'r_user_emb': r_user_emb, 'L0_rec_item_feature_matrix': _L0_rec_in['item_feature_matrix'], 'L0_rec_feat_w': _L0_rec_in['feat_w'], 'L0_rec_feat_b': _L0_rec_in['feat_b'], 'L0_rec_gcn_w': _L0_rec_in['gcn_w'], 'L0_rec_gcn_b': _L0_rec_in['gcn_b']}

def reference(r_user_item_matrix, r_user_emb, L0_rec_item_feature_matrix, L0_rec_feat_w, L0_rec_feat_b, L0_rec_gcn_w, L0_rec_gcn_b):
    import jax
    import jax.numpy as jnp

    def _L0_rec_ref(user_item_matrix, item_feature_matrix, user_emb, feat_w, feat_b, gcn_w, gcn_b):
        import jax, jax.numpy as jnp
        import numpy as np
        U, I, F, H = (1000, 750, 128, 64)
        R = user_item_matrix
        d_u = jnp.clip(1.0 + R.sum(axis=1), 1e-08) ** (-0.5)
        d_i = jnp.clip(1.0 + R.sum(axis=0), 1e-08) ** (-0.5)
        item_feats = item_feature_matrix @ feat_w + feat_b
        fu = d_u[:, None] * user_emb
        fi = d_i[:, None] * item_feats
        support_u = d_u[:, None] * (fu + R @ fi)
        support_i = d_i[:, None] * (fi + R.T @ fu)
        user_out = support_u @ gcn_w + gcn_b
        item_out = support_i @ gcn_w + gcn_b
        return user_out @ item_out.T
    y = _L0_rec_ref(r_user_item_matrix, L0_rec_item_feature_matrix, r_user_emb, L0_rec_feat_w, L0_rec_feat_b, L0_rec_gcn_w, L0_rec_gcn_b)
    return y

_drawn_inputs = setup_inputs


def setup_inputs(seed=0):
    import zlib

    import numpy as np

    out = dict(_drawn_inputs(seed))
    spreads = {}
    factors = {}
    for name, (base, spread) in spreads.items():
        noise = np.random.default_rng([zlib.crc32(name.encode()), seed]).standard_normal(out[name].shape)
        drawn = base * np.exp(spread * noise) if base else spread * noise
        out[name] = jnp.asarray(drawn.astype(out[name].dtype))
    for name, factor in factors.items():
        out[name] = (out[name] * factor).astype(out[name].dtype)
    return out
```

```python
from contextlib import ExitStack

import concourse.bass as bass
from concourse import mybir


def lightgcn_scores(
    nc: bass.Bass,
    ratings: bass.AP,
    user_emb: bass.AP,
    user_emb_T: bass.AP,
    item_feat_T: bass.AP,
    identity: bass.AP,
    feat_w_T: bass.AP,
    gcn_w_quad: bass.AP,
    feat_b_col: bass.AP,
    gcn_b_col: bass.AP,
    scores: bass.AP,
):
    f32, f32r = mybir.dt.float32, mybir.dt.float32r
    ALU, ACT, AX = mybir.AluOpType, mybir.ActivationFunctionType, mybir.AxisListType

    P = 128
    USERS, ITEMS = ratings.shape
    H = user_emb.shape[1]
    TILES = USERS // P
    CHUNKS = 6
    IC = ITEMS // CHUNKS
    HALF = ITEMS // 2
    HPAD = HALF + 1
    UNITS = 4
    UW = USERS // UNITS // 2
    LOADS = [(0, 1), (1, 1)] + [(t, 2) for t in range(2, TILES, 2)]
    GROUPS = [(0, 1), (1, 1), (2, 2)] + [(t, 4) for t in range(4, TILES, 4)]
    NG = len(GROUPS)
    FLOOR = 1e-8

    R_dram = ratings.rearrange("(p t) i -> p t i", p=P)
    E_dram = user_emb.rearrange("(p t) h -> p t h", p=P)
    Y_dram = scores.rearrange("(p t) i -> p t i", p=P)

    def load_of(tile):
        return next(n for n, (t, k) in enumerate(LOADS) if t <= tile < t + k)

    with ExitStack() as ctx:
        def sb(name, shape, dt=f32):
            return ctx.enter_context(nc.sbuf_tensor(name, shape, dt))

        def sem(name):
            return ctx.enter_context(nc.semaphore(name))

        R = sb("R", [P, TILES, ITEMS])
        RT = sb("RT", [IC, CHUNKS, USERS])
        Y = sb("Y", [P, TILES, ITEMS])
        ident = sb("ident", [P, P])
        E = sb("E", [P, TILES, H])
        ET = sb("ET", [P, UNITS, UW])
        FT = sb("FT", [P, ITEMS])
        fwT = sb("fwT", [H, P])
        WW = sb("WW", [P, P])
        WD = sb("WD", [P, P])
        fb = sb("fb", [H, 1])
        gb = sb("gb", [P, 1])
        FW = sb("FW", [P, 2 * H + 1])
        X = sb("X", [IC, CHUNKS, H])
        XT = sb("XT", [P, 2, HALF])
        half_neg = sb("half_neg", [P, TILES])
        rsum = sb("rsum", [P, TILES])
        rdeg = sb("rdeg", [P, TILES])
        du = sb("du", [P, TILES])
        duE = sb("duE", [P, TILES, H])
        csum = sb("csum", [IC, CHUNKS, NG])
        cdeg = sb("cdeg", [IC, CHUNKS])
        cdeg1 = sb("cdeg1", [IC, CHUNKS])
        di = sb("di", [IC, CHUNKS])
        diX = sb("diX", [IC, CHUNKS, H])
        DU = sb("DU", [P, UNITS, UW])
        DI = sb("DI", [P, 2, HALF])
        own_u = sb("own_u", [P, UNITS, UW])
        own_i = sb("own_i", [P, 2, HALF])
        AG = sb("AG", [P, 2, HALF])
        ms = sb("ms", [P, 2, UW])
        us = sb("us", [P, 2, UW])
        mv = sb("mv", [P, 2, HALF])
        vs = sb("vs", [P, 2, HALF])
        UO = sb("UO", [P, UNITS, 2, UW], f32r)
        Vh = sb("Vh", [P, 2, HPAD], f32r)
        Vl = sb("Vl", [P, 2, HPAD], f32r)

        PB = [ctx.enter_context(nc.psum_tensor(f"PB{i}", [P, 2, 512], f32)) for i in range(4)]

        s_load = [sem(f"s_load{n}") for n in range(len(LOADS))]
        s_ident, s_params, s_feat, s_E, s_ET = (sem(f"s_{n}") for n in ("ident", "params", "feat", "E", "ET"))
        s_wd0, s_wd, s_exp, s_pads = sem("s_wd0"), sem("s_wd"), sem("s_exp"), sem("s_pads")
        s_fw_mm, s_fw, s_x_mm, s_xt_mm, s_x, s_xt = (sem(f"s_{n}") for n in ("fw_mm", "fw", "x_mm", "xt_mm", "x", "xt"))
        s_rsum, s_rdeg, s_du, s_duE = (sem(f"s_{n}") for n in ("rsum", "rdeg", "du", "duE"))
        s_T, s_RT = sem("s_T"), sem("s_RT")
        s_cdeg, s_di, s_diX = sem("s_cdeg"), sem("s_di"), sem("s_diX")
        s_WE, s_DU_mm, s_DI_mm = sem("s_WE"), sem("s_DU_mm"), sem("s_DI_mm")
        s_DU, s_DI, s_own_u, s_own_i = sem("s_DU"), sem("s_DI"), sem("s_own_u"), sem("s_own_i")
        s_A, s_AG, s_WA = sem("s_A"), sem("s_AG"), sem("s_WA")
        s_B, s_ms, s_us, s_uhi, s_ulo = (sem(f"s_{n}") for n in ("B", "ms", "us", "uhi", "ulo"))
        s_mv, s_vs, s_vhi, s_vlo = (sem(f"s_{n}") for n in ("mv", "vs", "vhi", "vlo"))
        s_C, s_Y, s_stored = sem("s_C"), [sem("s_Y0"), sem("s_Y1")], sem("s_stored")

        block = ctx.enter_context(nc.Block())

        def by(t):
            return t % 2

        @block.sync
        def _(sp):
            for n, (t, k) in enumerate(LOADS):
                sp.dma_start(R[:, t:t + k, :], R_dram[:, t:t + k, :]).then_inc(s_load[n], 16)
            sp.dma_start(ET[:, :, :], user_emb_T.rearrange("p (q n) -> p q n", q=UNITS)).then_inc(s_ET, 16)
            for t in range(0, TILES, 2):
                for k in range(2):
                    sp.wait_ge(s_Y[k], t // 2 + 1)
                sp.dma_start(Y_dram[:, t:t + 2, :], Y[:, t:t + 2, :]).then_inc(s_stored, 16)
            sp.wait_ge(s_stored, 16 * (TILES // 2))

        @block.scalar
        def _(act):
            act.dma_start(ident[:, :], identity).then_inc(s_ident, 16)
            act.dma_start(fwT[:, :], feat_w_T).then_inc(s_params, 16)
            act.dma_start(WW[:, :], gcn_w_quad).then_inc(s_params, 16)
            act.dma_start(fb[:, :], feat_b_col).then_inc(s_params, 16)
            act.dma_start(gb[:, :], gcn_b_col).then_inc(s_params, 16)
            act.dma_start(E[:, :, :], E_dram).then_inc(s_E, 16)
            act.dma_start(FT[:, :], item_feat_T).then_inc(s_feat, 16)

            for g, (t, k) in enumerate(GROUPS):
                for c in range(CHUNKS):
                    act.wait_ge(s_T, CHUNKS * g + c + 1)
                    nc.scalar.activation(RT[:, c, t * P:(t + k) * P], PB[1 + c // 2][0:IC, c % 2, 0:k * P],
                                         ACT.Identity, accum_out=csum[:, c, g:g + 1]).then_inc(s_RT, 1)
            act.wait_ge(s_DU_mm, 1)
            nc.scalar.copy(DU[:, :, :], PB[2][:, :, :].rearrange("p b (u n) -> p (b u) n", u=2)).then_inc(s_DU, 1)
            act.wait_ge(s_DI_mm, 1)
            nc.scalar.copy(DI[:, :, :], PB[3][:, :, 0:HALF]).then_inc(s_DI, 1)
            act.wait_ge(s_A, 1)
            nc.scalar.copy(AG[:, :, :], PB[0][:, :, 0:HALF]).then_inc(s_AG, 1)

            def user_high(q):
                act.wait_ge(s_us, q + 1)
                for h in range(2):
                    rows = slice(H * h, H * h + H)
                    nc.scalar.activation(UO[rows, q, h, :], us[rows, q % 2, :], ACT.Identity,
                                         bias=gb[rows, :]).then_inc(s_uhi, 1)

            def out(t):
                act.wait_ge(s_C, t + 1)
                nc.scalar.copy(Y[:, t, :].rearrange("p (b i) -> p b i", b=2),
                               PB[(3, 0, 2)[t % 3]][:, :, 0:HALF]).then_inc(s_Y[1], 1)

            user_high(0)
            act.wait_ge(s_vs, 1)
            nc.scalar.activation(Vh[:, :, 0:HALF], vs[:, :, :], ACT.Identity, bias=gb[:, :]).then_inc(s_vhi, 1)
            for q in range(1, UNITS):
                user_high(q)
                for t in range(4 * q - 4, 4 * q):
                    if by(t) == 1:
                        out(t)
            for t in range(TILES - 4, TILES):
                if by(t) == 1:
                    out(t)

        @block.gpsimd
        def _(pool):
            nc.gpsimd.memset(half_neg[:, :], -0.5).then_inc(s_exp, 1)
            nc.gpsimd.memset(WD[:, :], 0.0).then_inc(s_wd0, 1)
            pool.wait_ge(s_params, 64)
            pool.wait_ge(s_wd0, 1)
            for h in range(2):
                b = slice(H * h, H * h + H)
                nc.gpsimd.tensor_copy(WD[b, b], WW[b, b]).then_inc(s_wd, 1)
            pool.wait_ge(s_wd, 2)
            pool.wait_ge(s_exp, 1)
            pool.wait_ge(s_E, 16)
            for n, (t, k) in enumerate(LOADS):
                pool.wait_ge(s_rdeg, n + 1)
                if n >= 1:
                    pool.wait_ge(s_duE, n)
                nc.gpsimd.tensor_tensor(du[:, t:t + k], rdeg[:, t:t + k], half_neg[:, t:t + k],
                                        ALU.pow).then_inc(s_du, 1)
                pool.wait_ge(s_du, n + 1)
                nc.gpsimd.tensor_tensor(duE[:, t:t + k, :], E[:, t:t + k, :],
                                        du[:, t:t + k].unsqueeze(2).to_broadcast([P, k, H]),
                                        ALU.mult).then_inc(s_duE, 1)
            pool.wait_ge(s_duE, len(LOADS))
            pool.wait_ge(s_cdeg, 2)
            nc.gpsimd.tensor_tensor(di[:, :], cdeg1[:, :], half_neg[0:IC, 0:CHUNKS], ALU.pow).then_inc(s_di, 1)
            pool.wait_ge(s_di, 1)
            pool.wait_ge(s_DI, 1)
            pool.wait_ge(s_xt, 2)
            nc.gpsimd.tensor_tensor(own_i[:, :, :], XT[:, :, :], DI[:, :, :], ALU.mult).then_inc(s_own_i, 1)

        @block.vector
        def _(dve):
            nc.vector.memset(Vh[:, :, HALF:HPAD].bitcast(f32), 0.0).then_inc(s_pads, 1)
            nc.vector.memset(Vl[:, :, HALF:HPAD].bitcast(f32), 0.0).then_inc(s_pads, 1)

            def degrees(n):
                t, k = LOADS[n]
                dve.wait_ge(s_load[n], 16)
                nc.vector.reduce_sum(rsum[:, t:t + k], R[:, t:t + k, :], AX.X).then_inc(s_rsum, 1)
                dve.wait_ge(s_rsum, n + 1)
                nc.vector.tensor_scalar(rdeg[:, t:t + k], rsum[:, t:t + k], 1.0, FLOOR,
                                        ALU.add, ALU.max).then_inc(s_rdeg, 1)

            degrees(0)
            dve.wait_ge(s_fw_mm, 1)
            nc.vector.tensor_copy(FW[:, :], PB[0][:, 0, 0:2 * H + 1]).then_inc(s_fw, 1)
            degrees(1)
            dve.wait_ge(s_fw, 1)
            dve.wait_ge(s_xt_mm, 1)
            nc.vector.tensor_scalar(XT[:, 0, :], PB[0][:, 0, 0:HALF], FW[:, 2 * H:2 * H + 1], None,
                                    ALU.add).then_inc(s_xt, 1)
            dve.wait_ge(s_x_mm, 1)
            nc.vector.tensor_tensor(X[:, :, :], PB[0][0:IC, 1, 0:CHUNKS * H].rearrange("p (c h) -> p c h", c=CHUNKS),
                                    FW[0:IC, H:2 * H].unsqueeze(1).to_broadcast([IC, CHUNKS, H]),
                                    ALU.add).then_inc(s_x, 1)
            degrees(2)
            dve.wait_ge(s_xt_mm, 2)
            nc.vector.tensor_scalar(XT[:, 1, :], PB[0][:, 1, 0:HALF], FW[:, 2 * H:2 * H + 1], None,
                                    ALU.add).then_inc(s_xt, 1)
            for n in range(3, len(LOADS)):
                degrees(n)

            dve.wait_ge(s_RT, NG * CHUNKS)
            nc.vector.reduce_sum(cdeg[:, :], csum[:, :, :], AX.X).then_inc(s_cdeg, 1)
            dve.wait_ge(s_cdeg, 1)
            nc.vector.tensor_scalar(cdeg1[:, :], cdeg[:, :], 1.0, FLOOR, ALU.add, ALU.max).then_inc(s_cdeg, 1)
            dve.wait_ge(s_di, 1)
            dve.wait_ge(s_x, 1)
            nc.vector.tensor_tensor(diX[:, :, :], X[:, :, :], di[:, :].unsqueeze(2).to_broadcast([IC, CHUNKS, H]),
                                    ALU.mult).then_inc(s_diX, 1)
            dve.wait_ge(s_DU, 1)
            dve.wait_ge(s_WE, 1)
            nc.vector.tensor_tensor(own_u[:, :, :], PB[1][:, :, :].rearrange("p b (u n) -> p (b u) n", u=2),
                                    DU[:, :, :], ALU.mult).then_inc(s_own_u, 1)

            def user_sums(q):
                dve.wait_ge(s_B, q + 1)
                dve.wait_ge(s_own_u, 1)
                nc.vector.tensor_tensor(ms[:, q % 2, :], PB[1][:, q % 2, UW * (q // 2):UW * (q // 2) + UW],
                                        own_u[:, q, :], ALU.add).then_inc(s_ms, 1)
                dve.wait_ge(s_ms, q + 1)
                if q >= 2:
                    dve.wait_ge(s_uhi, 2 * q - 2)
                nc.vector.tensor_tensor(us[:, q % 2, :], ms[:, q % 2, :], DU[:, q, :], ALU.mult).then_inc(s_us, 1)

            def user_low(q):
                dve.wait_ge(s_us, q + 1)
                for h in range(2):
                    dve.wait_ge(s_uhi, 2 * q + h + 1)
                    rows, other = slice(H * h, H * h + H), slice(H - H * h, 2 * H - H * h)
                    nc.vector.scalar_tensor_tensor(out=UO[other, q, h, :], in0=us[rows, q % 2, :],
                                                   scalar=gb[rows, :], in1=UO[rows, q, h, :].bitcast(f32),
                                                   op0=ALU.add, op1=ALU.subtract).then_inc(s_ulo, 1)

            def out(t):
                dve.wait_ge(s_C, t + 1)
                nc.vector.tensor_copy(Y[:, t, :].rearrange("p (b i) -> p b i", b=2),
                                      PB[(3, 0, 2)[t % 3]][:, :, 0:HALF]).then_inc(s_Y[0], 1)

            user_sums(0)
            dve.wait_ge(s_params, 64)
            user_low(0)
            dve.wait_ge(s_own_i, 1)
            dve.wait_ge(s_WA, 1)
            nc.vector.tensor_tensor(mv[:, :, :], PB[2][:, :, 0:HALF], own_i[:, :, :], ALU.add).then_inc(s_mv, 1)
            dve.wait_ge(s_mv, 1)
            nc.vector.tensor_tensor(vs[:, :, :], mv[:, :, :], DI[:, :, :], ALU.mult).then_inc(s_vs, 1)
            dve.wait_ge(s_vhi, 1)
            nc.vector.scalar_tensor_tensor(out=Vl[:, :, 0:HALF], in0=vs[:, :, :], scalar=gb[:, :],
                                           in1=Vh[:, :, 0:HALF].bitcast(f32),
                                           op0=ALU.add, op1=ALU.subtract).then_inc(s_vlo, 1)
            for q in range(1, UNITS):
                user_sums(q)
                user_low(q)
                for t in range(4 * q - 4, 4 * q):
                    if by(t) == 0:
                        out(t)
            for t in range(TILES - 4, TILES):
                if by(t) == 0:
                    out(t)

        @block.tensor
        def _(pe):
            def transposes(g):
                t, k = GROUPS[g]
                pe.wait_ge(s_load[load_of(t)], 16)
                if k > 2:
                    pe.wait_ge(s_load[load_of(t + k - 1)], 16)
                for c in range(CHUNKS):
                    if g >= 1:
                        pe.wait_ge(s_RT, CHUNKS * (g - 1) + c + 1)
                    for j in range(k):
                        last = nc.tensor.transpose(PB[1 + c // 2][0:IC, c % 2, j * P:(j + 1) * P],
                                                   R[:, t + j, c * IC:(c + 1) * IC], ident[:, :])
                    last.then_inc(s_T, 1)

            def aggregate(t):
                pe.wait_ge(s_duE, load_of(t + 1) + 1)
                for b in range(2):
                    for h in range(2):
                        last = nc.tensor.matmul(PB[0][H * h:H * h + H, b, 0:HALF], duE[:, t + h, :],
                                                R[:, t + h, b * HALF:(b + 1) * HALF],
                                                start=(t == 0), stop=(t == TILES - 2))
                if t == TILES - 2:
                    last.then_inc(s_A, 1)

            def propagate(q, chunks):
                for c in chunks:
                    for h in range(2):
                        u0 = (2 * q + h) * UW
                        last = nc.tensor.matmul(PB[1][H * h:H * h + H, q % 2, UW * (q // 2):UW * (q // 2) + UW],
                                                diX[:, c, :], RT[:, c, u0:u0 + UW],
                                                start=(c == 0), stop=(c == CHUNKS - 1))
                if chunks[-1] == CHUNKS - 1:
                    last.then_inc(s_B, 1)

            def score(t):
                q, h, j = t // 4, t // 2 % 2, t % 2
                pe.wait_ge(s_ulo, 2 * q + h + 1)
                if t >= 3:
                    pe.wait_ge(s_Y[by(t - 3)], (t - 3) // 2 + 1)
                for b in range(2):
                    for V in (Vh, Vl):
                        last = nc.tensor.matmul(PB[(3, 0, 2)[t % 3]][:, b, 0:HPAD], UO[:, q, h, j * P:(j + 1) * P],
                                                V[:, b, :], start=(V is Vh), stop=(V is Vl))
                last.then_inc(s_C, 1)

            pe.wait_ge(s_params, 64)
            nc.tensor.matmul(PB[0][:, 0, 0:H], fwT[:, :], WW[0:H, 0:H], start=True, stop=True)
            nc.tensor.matmul(PB[0][:, 0, H:2 * H], fb[:, :].to_broadcast([H, P]), WW[0:H, 0:H], start=True, stop=True)
            nc.tensor.matmul(PB[0][:, 0, 2 * H:2 * H + 1], WW[0:H, :], fb[:, :], start=True,
                             stop=True).then_inc(s_fw_mm, 1)
            pe.wait_ge(s_ident, 16)
            transposes(0)
            pe.wait_ge(s_feat, 16)
            pe.wait_ge(s_fw, 1)

            def x_columns(b):
                for h in range(2):
                    last = nc.tensor.matmul(PB[0][H * h:H * h + H, b, 0:HALF], FW[:, 0:H],
                                            FT[:, b * HALF:(b + 1) * HALF], start=True, stop=True)
                last.then_inc(s_xt_mm, 1)

            x_columns(0)
            for c in range(CHUNKS):
                last = nc.tensor.matmul(PB[0][0:IC, 1, c * H:(c + 1) * H], FT[:, c * IC:(c + 1) * IC], FW[:, 0:H],
                                        start=True, stop=True)
            last.then_inc(s_x_mm, 1)
            transposes(1)
            pe.wait_ge(s_x, 1)
            x_columns(1)
            transposes(2)
            pe.wait_ge(s_xt, 2)
            aggregate(0)
            transposes(3)
            aggregate(2)
            transposes(4)
            aggregate(4)
            aggregate(6)
            transposes(5)
            aggregate(8)
            pe.wait_ge(s_ET, 16)
            pe.wait_ge(s_wd, 2)
            pe.wait_ge(s_RT, CHUNKS * (NG - 1) + 2)
            for b in range(2):
                last = nc.tensor.matmul(PB[1][:, b, :], WD[:, :],
                                        ET[:, 2 * b:2 * b + 2, :].rearrange("p u n -> p (u n)"), start=True, stop=True)
            last.then_inc(s_WE, 1)
            pe.wait_ge(s_du, len(LOADS))
            pe.wait_ge(s_RT, CHUNKS * (NG - 1) + 4)
            for q in range(UNITS):
                for j in range(2):
                    for h in range(2):
                        t = 4 * q + 2 * h + j
                        at = UW * (q % 2) + P * j
                        last = nc.tensor.matmul(PB[2][H * h:H * h + H, q // 2, at:at + P],
                                                du[:, t:t + 1].to_broadcast([P, H]), ident[:, :],
                                                start=True, stop=True)
            last.then_inc(s_DU_mm, 1)
            aggregate(10)
            pe.wait_ge(s_di, 1)
            for c in range(CHUNKS):
                at = IC * (c % 3)
                last = nc.tensor.matmul(PB[3][:, c // 3, at:at + IC], di[:, c:c + 1].to_broadcast([IC, P]),
                                        ident[0:IC, 0:IC], start=True, stop=True)
            last.then_inc(s_DI_mm, 1)
            aggregate(12)
            aggregate(14)
            pe.wait_ge(s_diX, 1)
            pe.wait_ge(s_own_u, 1)
            propagate(0, [0, 1])
            pe.wait_ge(s_AG, 1)
            pe.wait_ge(s_DU, 1)
            for b in range(2):
                last = nc.tensor.matmul(PB[2][:, b, 0:HALF], WW[:, :], AG[:, b, :], start=True, stop=True)
            last.then_inc(s_WA, 1)
            propagate(0, [2, 3, 4, 5])
            propagate(1, list(range(CHUNKS)))
            pe.wait_ge(s_pads, 2)
            pe.wait_ge(s_vlo, 1)
            for q in range(UNITS):
                for t in range(4 * q, 4 * q + 4):
                    score(t)
                if q + 2 < UNITS:
                    pe.wait_ge(s_ms, q + 1)
                    propagate(q + 2, list(range(CHUNKS)))


def kernel(r_user_item_matrix, r_user_emb, L0_rec_item_feature_matrix, L0_rec_feat_w, L0_rec_feat_b,
           L0_rec_gcn_w, L0_rec_gcn_b):
    import numpy as np
    import concourse.bacc as bacc
    from concourse.bass_utils import run_bass_kernel_spmd

    ratings, emb, feats, feat_w, feat_b, gcn_w, gcn_b = (
        np.asarray(a) for a in (r_user_item_matrix, r_user_emb, L0_rec_item_feature_matrix, L0_rec_feat_w,
                                L0_rec_feat_b, L0_rec_gcn_w, L0_rec_gcn_b))
    users, items = ratings.shape
    hidden = emb.shape[1]
    emb_T = emb.reshape(128, 4, 2, 2, hidden).transpose(2, 4, 1, 3, 0).reshape(2 * hidden, users // 2)
    arrays = {
        "ratings": ratings,
        "user_emb": emb,
        "user_emb_T": emb_T,
        "item_feat_T": feats.T,
        "identity": np.eye(128, dtype=np.float32),
        "feat_w_T": feat_w.T,
        "gcn_w_quad": np.tile(gcn_w, (2, 2)),
        "feat_b_col": feat_b.reshape(hidden, 1),
        "gcn_b_col": np.tile(gcn_b, 2).reshape(2 * hidden, 1),
    }
    arrays = {name: np.ascontiguousarray(a) for name, a in arrays.items()}
    nc = bacc.Bacc("TRN2", target_bir_lowering=False, num_devices=1)
    args = [nc.dram_tensor(name, a.shape, mybir.dt.from_np(a.dtype), kind="ExternalInput").ap()
            for name, a in arrays.items()]
    out = nc.dram_tensor("scores", (users, items), mybir.dt.float32, kind="ExternalOutput").ap()
    lightgcn_scores(nc, *args, out)
    result = run_bass_kernel_spmd(nc, [arrays], core_ids=[0])
    return result.results[0]["scores"]
```

```python
from contextlib import ExitStack

import concourse.bass as bass
from concourse import mybir


def lightgcn_scores(
    nc: bass.Bass,
    ratings: bass.AP,
    user_emb: bass.AP,
    user_emb_T: bass.AP,
    item_feat_T: bass.AP,
    small: bass.AP,
    scores: bass.AP,
):
    f32, f32r = mybir.dt.float32, mybir.dt.float32r
    ALU, ACT, AX = mybir.AluOpType, mybir.ActivationFunctionType, mybir.AxisListType

    P = 128
    USERS, ITEMS = ratings.shape
    H = user_emb.shape[1]
    TILES = USERS // P
    CHUNKS = 6
    IC = ITEMS // CHUNKS
    HALF = ITEMS // 2
    HPAD = HALF + 1
    UNITS = 4
    UW = USERS // UNITS // 2
    LOADS = [(0, 1), (1, 1)] + [(t, 2) for t in range(2, TILES, 2)]
    GROUPS = [(0, 1), (1, 1), (2, 2)] + [(t, 4) for t in range(4, TILES, 4)]
    NG = len(GROUPS)
    FLOOR = 1e-8

    R_dram = ratings.rearrange("(p t) i -> p t i", p=P)
    E_dram = user_emb.rearrange("(p t) h -> p t h", p=P)
    Y_dram = scores.rearrange("(p t) i -> p t i", p=P)

    def load_of(tile):
        return next(n for n, (t, k) in enumerate(LOADS) if t <= tile < t + k)

    with ExitStack() as ctx:
        def sb(name, shape, dt=f32):
            return ctx.enter_context(nc.sbuf_tensor(name, shape, dt))

        def sem(name):
            return ctx.enter_context(nc.semaphore(name))

        R = sb("R", [P, TILES, ITEMS])
        RT = sb("RT", [IC, CHUNKS, USERS])
        Y = sb("Y", [P, TILES, ITEMS])
        S = sb("S", [P, small.shape[1]])
        E = sb("E", [P, TILES, H])
        ET = sb("ET", [P, UNITS, UW])
        FT = sb("FT", [P, ITEMS])
        WD = sb("WD", [P, P])
        ident, WW, fwT = S[:, 0:P], S[:, P:2 * P], S[0:H, 2 * P:3 * P]
        gb, fb = S[:, 3 * P:3 * P + 1], S[0:H, 3 * P + 1:3 * P + 2]
        FW = sb("FW", [P, 2 * H])
        X = sb("X", [IC, CHUNKS, H])
        half_neg = sb("half_neg", [P, TILES])
        rsum = sb("rsum", [P, TILES])
        rdeg = sb("rdeg", [P, TILES])
        du = sb("du", [P, TILES])
        duE = sb("duE", [P, TILES, H])
        csum = sb("csum", [IC, CHUNKS, NG])
        cdeg = sb("cdeg", [IC, CHUNKS])
        cdeg1 = sb("cdeg1", [IC, CHUNKS])
        di = sb("di", [IC, CHUNKS])
        diX = sb("diX", [IC, CHUNKS, 2, H])
        DU = sb("DU", [P, UNITS, UW])
        DI = sb("DI", [P, 2, HALF])
        duT = sb("duT", [TILES, P])
        duET = sb("duET", [P, UNITS, UW])
        AG = sb("AG", [P, 2, HALF])
        us = sb("us", [P, 2, UW])
        vs = sb("vs", [P, 2, HALF])
        UO = sb("UO", [P, UNITS, 2, UW], f32r)
        Vh = sb("Vh", [P, 2, HPAD], f32r)
        Vl = sb("Vl", [P, 2, HPAD], f32r)

        PB = [ctx.enter_context(nc.psum_tensor(f"PB{i}", [P, 2, 512], f32)) for i in range(4)]

        s_load = [sem(f"s_load{n}") for n in range(len(LOADS))]
        s_small, s_feat, s_E, s_ET = (sem(f"s_{n}") for n in ("small", "feat", "E", "ET"))
        s_wd0, s_wd, s_exp, s_pads = sem("s_wd0"), sem("s_wd"), sem("s_exp"), sem("s_pads")
        s_fw_mm, s_fw, s_x_mm, s_x = (sem(f"s_{n}") for n in ("fw_mm", "fw", "x_mm", "x"))
        s_rsum, s_rdeg, s_du, s_duE = (sem(f"s_{n}") for n in ("rsum", "rdeg", "du", "duE"))
        s_T, s_RT = sem("s_T"), sem("s_RT")
        s_cdeg, s_di, s_diX = sem("s_cdeg"), sem("s_di"), sem("s_diX")
        s_duT_mm, s_duT, s_du_out, s_DU, s_duET = (sem(f"s_{n}") for n in ("duT_mm", "duT", "du_out", "DU", "duET"))
        s_DI_mm, s_DI = sem("s_DI_mm"), sem("s_DI")
        s_A, s_AG, s_V = sem("s_A"), sem("s_AG"), sem("s_V")
        s_B, s_us, s_uhi, s_ulo = (sem(f"s_{n}") for n in ("B", "us", "uhi", "ulo"))
        s_vs, s_vhi, s_vlo = (sem(f"s_{n}") for n in ("vs", "vhi", "vlo"))
        s_C, s_Y, s_stored = sem("s_C"), [sem("s_Y0"), sem("s_Y1")], sem("s_stored")

        du_dram = nc.dram_tensor("du_rows", (TILES, P), f32, kind="Internal").ap()

        block = ctx.enter_context(nc.Block())

        def by(t):
            return t % 2

        TURN = [1, 0, 1, 1] * 3 + [0, 1, 0, 1]

        def moved(t):
            return TURN[:t + 1].count(TURN[t])

        SCORES = (3, 0, 2)

        @block.sync
        def _(sp):
            sp.dma_start(S[:, :], small).then_inc(s_small, 16)
            sp.dma_start(FT[:, :], item_feat_T).then_inc(s_feat, 16)
            for n, (t, k) in enumerate(LOADS):
                sp.dma_start(R[:, t:t + k, :], R_dram[:, t:t + k, :]).then_inc(s_load[n], 16)
                if n == 1:
                    sp.dma_start(E[:, :, :], E_dram).then_inc(s_E, 16)
            sp.dma_start(ET[:, :, :], user_emb_T.rearrange("p (q n) -> p q n", q=UNITS)).then_inc(s_ET, 16)
            sp.wait_ge(s_duT, 1)
            sp.dma_start(du_dram, duT[:, :]).then_inc(s_du_out, 16)
            sp.wait_ge(s_du_out, 16)
            by_half = du_dram.rearrange("(q h j) p -> h q (j p)", q=UNITS, h=2)
            for h in range(2):
                sp.dma_start(DU[H * h:H * h + H, :, :],
                             by_half[h:h + 1].to_broadcast([H, UNITS, UW])).then_inc(s_DU, 16)
            for t in range(0, TILES, 2):
                for k in range(2):
                    if TURN[:t + 2].count(k):
                        sp.wait_ge(s_Y[k], TURN[:t + 2].count(k))
                sp.dma_start(Y_dram[:, t:t + 2, :], Y[:, t:t + 2, :]).then_inc(s_stored, 16)
            sp.wait_ge(s_stored, 16 * (TILES // 2))

        def move_scores(eng, copy, t):
            eng.wait_ge(s_C, t + 1)
            copy(Y[:, t, :].rearrange("p (b i) -> p b i", b=2),
                 PB[SCORES[t % 3]][:, :, 0:HALF]).then_inc(s_Y[TURN[t]], 1)

        @block.scalar
        def _(act):
            for g, (t, k) in enumerate(GROUPS):
                for c in range(CHUNKS):
                    act.wait_ge(s_T, CHUNKS * g + c + 1)
                    nc.scalar.activation(RT[:, c, t * P:(t + k) * P], PB[1 + c // 2][0:IC, c % 2, 0:k * P],
                                         ACT.Identity, accum_out=csum[:, c, g:g + 1]).then_inc(s_RT, 1)
            act.wait_ge(s_DI_mm, 1)
            nc.scalar.copy(DI[:, :, :], PB[3][:, :, 0:HALF]).then_inc(s_DI, 1)

            def user_high(q):
                act.wait_ge(s_us, q + 1)
                for h in range(2):
                    rows = slice(H * h, H * h + H)
                    nc.scalar.activation(UO[rows, q, h, :], us[rows, q % 2, :], ACT.Identity,
                                         bias=gb[rows, :]).then_inc(s_uhi, 1)

            user_high(0)
            act.wait_ge(s_A, 1)
            nc.scalar.copy(AG[:, 0, :], PB[0][:, 0, 0:HALF]).then_inc(s_AG, 1)
            for b in range(2):
                act.wait_ge(s_vs, b + 1)
                nc.scalar.activation(Vh[:, b, 0:HALF], vs[:, b, :], ACT.Identity, bias=gb[:, :]).then_inc(s_vhi, 1)
            for q in range(1, UNITS + 1):
                if q < UNITS:
                    user_high(q)
                for t in range(4 * q - 4, 4 * q):
                    if TURN[t] == 1:
                        move_scores(act, nc.scalar.copy, t)

        @block.gpsimd
        def _(pool):
            nc.gpsimd.memset(half_neg[:, :], -0.5).then_inc(s_exp, 1)
            nc.gpsimd.memset(WD[:, :], 0.0).then_inc(s_wd0, 1)
            pool.wait_ge(s_small, 16)
            pool.wait_ge(s_wd0, 1)
            for h in range(2):
                b = slice(H * h, H * h + H)
                nc.gpsimd.tensor_copy(WD[b, b], WW[b, b]).then_inc(s_wd, 1)
            pool.wait_ge(s_wd, 2)
            pool.wait_ge(s_exp, 1)
            pool.wait_ge(s_E, 16)
            for n, (t, k) in enumerate(LOADS):
                pool.wait_ge(s_rdeg, n + 1)
                if n >= 1:
                    pool.wait_ge(s_duE, n)
                nc.gpsimd.tensor_tensor(du[:, t:t + k], rdeg[:, t:t + k], half_neg[:, t:t + k],
                                        ALU.pow).then_inc(s_du, 1)
                pool.wait_ge(s_du, n + 1)
                nc.gpsimd.tensor_tensor(duE[:, t:t + k, :], E[:, t:t + k, :],
                                        du[:, t:t + k].unsqueeze(2).to_broadcast([P, k, H]),
                                        ALU.mult).then_inc(s_duE, 1)
            pool.wait_ge(s_duE, len(LOADS))
            pool.wait_ge(s_cdeg, 2)
            nc.gpsimd.tensor_tensor(di[:, :], cdeg1[:, :], half_neg[0:IC, 0:CHUNKS], ALU.pow).then_inc(s_di, 1)
            pool.wait_ge(s_di, 1)
            pool.wait_ge(s_ET, 16)
            pool.wait_ge(s_DU, 32)
            for q in range(UNITS):
                if q >= 1:
                    pool.wait_ge(s_duET, q)
                nc.gpsimd.tensor_tensor(duET[:, q, :], ET[:, q, :], DU[:, q, :], ALU.mult).then_inc(s_duET, 1)

        @block.vector
        def _(dve):
            nc.vector.memset(Vh[:, :, HALF:HPAD].bitcast(f32), 0.0).then_inc(s_pads, 1)
            nc.vector.memset(Vl[:, :, HALF:HPAD].bitcast(f32), 0.0).then_inc(s_pads, 1)

            def degrees(n):
                t, k = LOADS[n]
                dve.wait_ge(s_load[n], 16)
                nc.vector.reduce_sum(rsum[:, t:t + k], R[:, t:t + k, :], AX.X).then_inc(s_rsum, 1)
                dve.wait_ge(s_rsum, n + 1)
                nc.vector.tensor_scalar(rdeg[:, t:t + k], rsum[:, t:t + k], 1.0, FLOOR,
                                        ALU.add, ALU.max).then_inc(s_rdeg, 1)

            dve.wait_ge(s_fw_mm, 1)
            nc.vector.tensor_copy(FW[:, :], PB[0][:, 0, 0:2 * H]).then_inc(s_fw, 1)
            dve.wait_ge(s_fw, 1)
            dve.wait_ge(s_x_mm, 1)
            nc.vector.tensor_tensor(X[:, :, :], PB[0][0:IC, 1, 0:CHUNKS * H].rearrange("p (c h) -> p c h", c=CHUNKS),
                                    FW[0:IC, H:2 * H].unsqueeze(1).to_broadcast([IC, CHUNKS, H]),
                                    ALU.add).then_inc(s_x, 1)
            for n in range(len(LOADS)):
                degrees(n)
            dve.wait_ge(s_duT_mm, 1)
            nc.vector.tensor_copy(duT[:, :], PB[1][0:TILES, 0, 0:P]).then_inc(s_duT, 1)

            dve.wait_ge(s_RT, NG * CHUNKS)
            nc.vector.reduce_sum(cdeg[:, :], csum[:, :, :], AX.X).then_inc(s_cdeg, 1)
            dve.wait_ge(s_cdeg, 1)
            nc.vector.tensor_scalar(cdeg1[:, :], cdeg[:, :], 1.0, FLOOR, ALU.add, ALU.max).then_inc(s_cdeg, 1)
            dve.wait_ge(s_di, 1)
            dve.wait_ge(s_x, 1)
            for a in range(2):
                nc.vector.tensor_tensor(diX[:, :, a, :], X[:, :, :],
                                        di[:, :].unsqueeze(2).to_broadcast([IC, CHUNKS, H]),
                                        ALU.mult).then_inc(s_diX, 1)

            def user_scaled(q):
                dve.wait_ge(s_B, q + 1)
                if q == 0:
                    dve.wait_ge(s_DU, 32)
                if q >= 2:
                    dve.wait_ge(s_uhi, 2 * q - 2)
                nc.vector.tensor_tensor(us[:, q % 2, :], PB[1][:, q % 2, UW * (q // 2):UW * (q // 2) + UW],
                                        DU[:, q, :], ALU.mult).then_inc(s_us, 1)

            def user_low(q):
                dve.wait_ge(s_us, q + 1)
                for h in range(2):
                    dve.wait_ge(s_uhi, 2 * q + h + 1)
                    rows, other = slice(H * h, H * h + H), slice(H - H * h, 2 * H - H * h)
                    nc.vector.scalar_tensor_tensor(out=UO[other, q, h, :], in0=us[rows, q % 2, :],
                                                   scalar=gb[rows, :], in1=UO[rows, q, h, :].bitcast(f32),
                                                   op0=ALU.add, op1=ALU.subtract).then_inc(s_ulo, 1)

            user_scaled(0)
            dve.wait_ge(s_small, 16)
            user_low(0)
            dve.wait_ge(s_A, 1)
            nc.vector.tensor_copy(AG[:, 1, :], PB[0][:, 1, 0:HALF]).then_inc(s_AG, 1)
            dve.wait_ge(s_DI, 1)
            for b in range(2):
                dve.wait_ge(s_V, b + 1)
                nc.vector.tensor_tensor(vs[:, b, :], PB[2][:, b, 0:HALF], DI[:, b, :], ALU.mult).then_inc(s_vs, 1)
            for b in range(2):
                dve.wait_ge(s_vhi, b + 1)
                nc.vector.scalar_tensor_tensor(out=Vl[:, b, 0:HALF], in0=vs[:, b, :], scalar=gb[:, :],
                                               in1=Vh[:, b, 0:HALF].bitcast(f32),
                                               op0=ALU.add, op1=ALU.subtract).then_inc(s_vlo, 1)
            for q in range(1, UNITS + 1):
                if q < UNITS:
                    user_scaled(q)
                    user_low(q)
                for t in range(4 * q - 4, 4 * q):
                    if TURN[t] == 0:
                        move_scores(dve, nc.vector.tensor_copy, t)

        @block.tensor
        def _(pe):
            def transposes(g):
                t, k = GROUPS[g]
                for n in range(load_of(t), load_of(t + k - 1) + 1):
                    pe.wait_ge(s_load[n], 16)
                for c in range(CHUNKS):
                    if g >= 1:
                        pe.wait_ge(s_RT, CHUNKS * (g - 1) + c + 1)
                    for j in range(k):
                        last = nc.tensor.transpose(PB[1 + c // 2][0:IC, c % 2, j * P:(j + 1) * P],
                                                   R[:, t + j, c * IC:(c + 1) * IC], ident)
                    last.then_inc(s_T, 1)

            def aggregate(t):
                pe.wait_ge(s_duE, load_of(t + 1) + 1)
                for b in range(2):
                    for h in range(2):
                        last = nc.tensor.matmul(PB[0][H * h:H * h + H, b, 0:HALF], duE[:, t + h, :],
                                                R[:, t + h, b * HALF:(b + 1) * HALF],
                                                start=(t == 0), stop=(t == TILES - 2))
                if t == TILES - 2:
                    last.then_inc(s_A, 1)

            def propagate(q, chunks):
                out = PB[1][:, q % 2, UW * (q // 2):UW * (q // 2) + UW]
                for c in chunks:
                    for h in range(2):
                        u0 = (2 * q + h) * UW
                        nc.tensor.matmul(out[H * h:H * h + H, :], diX[:, c, 0, :], RT[:, c, u0:u0 + UW],
                                         start=(c == 0), stop=False, skip_group_check=True)
                if chunks[-1] == CHUNKS - 1:
                    pe.wait_ge(s_duET, q + 1)
                    nc.tensor.matmul(out, WD[:, :], duET[:, q, :], start=False, stop=True,
                                     skip_group_check=True).then_inc(s_B, 1)

            def score(t):
                q, h, j = t // 4, t // 2 % 2, t % 2
                pe.wait_ge(s_ulo, 2 * q + h + 1)
                if t >= 3:
                    pe.wait_ge(s_Y[TURN[t - 3]], moved(t - 3))
                for b in range(2):
                    for V in (Vh, Vl):
                        if t == 0:
                            pe.wait_ge(s_vhi if V is Vh else s_vlo, b + 1)
                        last = nc.tensor.matmul(PB[SCORES[t % 3]][:, b, 0:HPAD], UO[:, q, h, j * P:(j + 1) * P],
                                                V[:, b, :], start=(V is Vh), stop=(V is Vl))
                last.then_inc(s_C, 1)

            pe.wait_ge(s_small, 16)
            nc.tensor.matmul(PB[0][:, 0, 0:H], fwT, WW[0:H, 0:H], start=True, stop=True)
            nc.tensor.matmul(PB[0][:, 0, H:2 * H], fb.to_broadcast([H, P]), WW[0:H, 0:H], start=True,
                             stop=True).then_inc(s_fw_mm, 1)
            pe.wait_ge(s_feat, 16)
            pe.wait_ge(s_fw, 1)
            for c in range(CHUNKS):
                last = nc.tensor.matmul(PB[0][0:IC, 1, c * H:(c + 1) * H], FT[:, c * IC:(c + 1) * IC], FW[:, 0:H],
                                        start=True, stop=True)
            last.then_inc(s_x_mm, 1)
            transposes(0)
            transposes(1)
            transposes(2)
            pe.wait_ge(s_x, 1)
            aggregate(0)
            aggregate(2)
            transposes(3)
            aggregate(4)
            transposes(4)
            aggregate(6)
            transposes(5)
            pe.wait_ge(s_du, len(LOADS))
            pe.wait_ge(s_RT, CHUNKS * (NG - 1) + 1)
            nc.tensor.transpose(PB[1][0:TILES, 0, 0:P], du[:, :], ident).then_inc(s_duT_mm, 1)
            aggregate(8)
            aggregate(10)
            pe.wait_ge(s_di, 1)
            for c in range(CHUNKS):
                at = IC * (c % 3)
                last = nc.tensor.matmul(PB[3][:, c // 3, at:at + IC], di[:, c:c + 1].to_broadcast([IC, P]),
                                        ident[0:IC, 0:IC], start=True, stop=True)
            last.then_inc(s_DI_mm, 1)
            pe.wait_ge(s_diX, 2)
            for c in range(CHUNKS):
                at = IC * (c % 3)
                nc.tensor.matmul(PB[2][:, c // 3, at:at + IC],
                                 diX[:, c, :, :].rearrange("p a h -> p (a h)"),
                                 ident[0:IC, 0:IC], start=(c % 3 == 0), stop=False, skip_group_check=True)
            pe.wait_ge(s_duT, 1)
            pe.wait_ge(s_wd, 2)
            propagate(0, list(range(CHUNKS)))
            aggregate(12)
            aggregate(14)
            propagate(1, [0])
            pe.wait_ge(s_AG, 2)
            for b in range(2):
                nc.tensor.matmul(PB[2][:, b, 0:HALF], WW[:, :], AG[:, b, :], start=False, stop=True,
                                 skip_group_check=True).then_inc(s_V, 1)
            propagate(1, list(range(1, CHUNKS)))
            pe.wait_ge(s_pads, 2)
            pe.wait_ge(s_DI, 1)
            for q in range(UNITS):
                for k in range(4):
                    score(4 * q + k)
                    if q + 2 < UNITS:
                        if k == 0:
                            pe.wait_ge(s_us, q + 1)
                        propagate(q + 2, [[0, 1], [2], [3, 4], [5]][k])


def kernel(r_user_item_matrix, r_user_emb, L0_rec_item_feature_matrix, L0_rec_feat_w, L0_rec_feat_b,
           L0_rec_gcn_w, L0_rec_gcn_b):
    import numpy as np
    import concourse.bacc as bacc
    from concourse.bass_utils import run_bass_kernel_spmd

    ratings, emb, feats, feat_w, feat_b, gcn_w, gcn_b = (
        np.asarray(a) for a in (r_user_item_matrix, r_user_emb, L0_rec_item_feature_matrix, L0_rec_feat_w,
                                L0_rec_feat_b, L0_rec_gcn_w, L0_rec_gcn_b))
    users, items = ratings.shape
    hidden = emb.shape[1]
    emb_T = emb.reshape(128, 4, 2, 2, hidden).transpose(2, 4, 1, 3, 0).reshape(2 * hidden, users // 2)
    small = np.zeros((128, 3 * 128 + 2), dtype=ratings.dtype)
    small[:, 0:128] = np.eye(128)
    small[:, 128:256] = np.tile(gcn_w, (2, 2))
    small[0:hidden, 256:384] = feat_w.T
    small[:, 384] = np.tile(gcn_b, 2)
    small[0:hidden, 385] = feat_b
    arrays = {"ratings": ratings, "user_emb": emb, "user_emb_T": emb_T, "item_feat_T": feats.T, "small": small}
    arrays = {name: np.ascontiguousarray(a) for name, a in arrays.items()}
    nc = bacc.Bacc("TRN2", target_bir_lowering=False, num_devices=1)
    args = [nc.dram_tensor(name, a.shape, mybir.dt.from_np(a.dtype), kind="ExternalInput").ap()
            for name, a in arrays.items()]
    out = nc.dram_tensor("scores", (users, items), mybir.dt.float32, kind="ExternalOutput").ap()
    lightgcn_scores(nc, *args, out)
    result = run_bass_kernel_spmd(nc, [arrays], core_ids=[0])
    return result.results[0]["scores"]
```

```python
from contextlib import ExitStack

import concourse.bass as bass
from concourse import mybir


def lightgcn_scores(
    nc: bass.Bass,
    ratings: bass.AP,
    user_emb: bass.AP,
    user_emb_T: bass.AP,
    item_feat_T: bass.AP,
    small: bass.AP,
    scores: bass.AP,
):
    f32, f32r = mybir.dt.float32, mybir.dt.float32r
    ALU, ACT, AX = mybir.AluOpType, mybir.ActivationFunctionType, mybir.AxisListType

    P = 128
    USERS, ITEMS = ratings.shape
    H = user_emb.shape[1]
    TILES = USERS // P
    CHUNKS = 6
    IC = ITEMS // CHUNKS
    HALF = ITEMS // 2
    HPAD = HALF + 1
    UNITS = 4
    UW = USERS // UNITS // 2
    PARTS = [(0, 0, UW), (1, 0, UW), (2, 0, UW), (3, 0, P), (3, P, P)]
    ORDER = list(range(TILES - 4)) + [TILES - 4, TILES - 2, TILES - 3, TILES - 1]
    LOADS = [(t, 1) for t in range(4)] + [(t, 2) for t in range(4, TILES, 2)]
    NL = len(LOADS)
    EG = 4
    E_AFTER = [1, 4, 5, 6]
    FLOOR = 1e-8

    R_dram = ratings.rearrange("(p t) i -> p t i", p=P)
    E_dram = user_emb.rearrange("(p t) h -> p t h", p=P)
    Y_dram = scores.rearrange("(p t) i -> p t i", p=P)

    def load_of(tile):
        return next(n for n, (t, k) in enumerate(LOADS) if t <= tile < t + k)

    def du_column(tile):
        return tile // 2 % 2 * (TILES // 2) + tile // 4 * 2 + tile % 2

    with ExitStack() as ctx:
        def sb(name, shape, dt=f32):
            return ctx.enter_context(nc.sbuf_tensor(name, shape, dt))

        def sem(name):
            return ctx.enter_context(nc.semaphore(name))

        R = sb("R", [P, TILES, ITEMS])
        RT = sb("RT", [IC, CHUNKS, USERS])
        Y = sb("Y", [P, TILES, ITEMS])
        S = sb("S", [P, small.shape[1]])
        E = sb("E", [P, TILES, H])
        ET = sb("ET", [P, UNITS, UW])
        FT = sb("FT", [P, ITEMS])
        zeros = sb("zeros", [P, 1], mybir.dt.bfloat16)
        WD = sb("WD", [P, P])
        ident, WW, fwT = S[:, 0:P], S[:, P:2 * P], S[0:H, 2 * P:3 * P]
        gb, fb = S[:, 3 * P:3 * P + 1], S[0:H, 3 * P + 1:3 * P + 2]
        FW = sb("FW", [P, H + 1])
        XT = sb("XT", [P, HALF])
        half_neg = sb("half_neg", [P, TILES])
        rsum = sb("rsum", [P, TILES])
        rdeg = sb("rdeg", [P, TILES])
        du = sb("du", [P, TILES])
        duE = sb("duE", [P, TILES, H])
        csum = sb("csum", [IC, CHUNKS, NL])
        cdeg = sb("cdeg", [IC, CHUNKS])
        cdeg1 = sb("cdeg1", [IC, CHUNKS])
        di = sb("di", [IC, CHUNKS])
        diX = sb("diX", [IC, CHUNKS, H])
        diXT = sb("diXT", [P, 2, HALF])
        vd = sb("vd", [P, 2, HALF])
        DU = sb("DU", [P, UNITS, UW])
        DI = sb("DI", [P, 2, HALF])
        duT = sb("duT", [TILES, P])
        duET = sb("duET", [P, UNITS, UW])
        AG = sb("AG", [P, 2, HALF])
        us = sb("us", [P, 2, UW])
        ub = sb("ub", [P, UW])
        vs = sb("vs", [P, 2, HALF])
        UO = sb("UO", [P, UNITS, 2, UW], f32r)
        Vh = sb("Vh", [P, 2, HPAD], f32r)
        Vl = sb("Vl", [P, 2, HPAD], f32r)

        PB = [ctx.enter_context(nc.psum_tensor(f"PB{i}", [P, 2, 512], f32)) for i in range(4)]

        s_load = [sem(f"s_load{n}") for n in range(NL)]
        s_small, s_feat, s_ET = (sem(f"s_{n}") for n in ("small", "feat", "ET"))
        s_E = [sem(f"s_E{a}") for a in range(TILES // EG)]
        s_zeros = sem("s_zeros")
        s_wd0, s_wd, s_exp, s_pads = sem("s_wd0"), sem("s_wd"), sem("s_exp"), sem("s_pads")
        s_fw_mm, s_fw, s_x_mm, s_x, s_xt = (sem(f"s_{n}") for n in ("fw_mm", "fw", "x_mm", "x", "xt"))
        s_diXT, s_vd = [sem("s_diXT0"), sem("s_diXT1")], sem("s_vd")
        s_rsum, s_rdeg, s_du, s_duE = (sem(f"s_{n}") for n in ("rsum", "rdeg", "du", "duE"))
        s_T, s_RT = sem("s_T"), sem("s_RT")
        s_cdeg, s_di, s_diX = sem("s_cdeg"), sem("s_di"), sem("s_diX")
        s_duT_mm, s_duT, s_du_out, s_DU0, s_duET = (sem(f"s_{n}") for n in ("duT_mm", "duT", "du_out", "DU0", "duET"))
        s_DU = sem("s_DU")
        s_DI_mm, s_DI = sem("s_DI_mm"), sem("s_DI")
        s_A, s_AG, s_V = sem("s_A"), [sem("s_AG0"), sem("s_AG1")], sem("s_V")
        s_B, s_us, s_ub = sem("s_B"), sem("s_us"), sem("s_ub")
        s_uhi, s_ulo = ([sem(f"s_{n}{h}") for h in range(2)] for n in ("uhi", "ulo"))
        s_vs, s_vhi, s_vlo = (sem(f"s_{n}") for n in ("vs", "vhi", "vlo"))
        s_C, s_Y, s_stored = sem("s_C"), {"A": sem("s_YA"), "V": sem("s_YV")}, sem("s_stored")

        du_dram = nc.dram_tensor("du_rows", (TILES, P), f32, kind="Internal").ap()

        block = ctx.enter_context(nc.Block())

        MOVERS = ["AA" if n in (2, 4, 13, 14) else "AV" for n in range(TILES)]

        def moved(n, b):
            engine = MOVERS[n][b]
            return s_Y[engine], "".join(MOVERS)[:2 * n + b + 1].count(engine)

        def part_of(t):
            return next(p for p, (q, u, w) in enumerate(PARTS) if q == t // 4 and u <= t % 2 * P < u + w)

        ROTATION = [3, 0, 2]
        BEFORE = [0, 0, 4, 9, 13]

        @block.sync
        def _(sp):
            sp.dma_start(S[:, :], small).then_inc(s_small, 16)
            for n, (t, k) in enumerate(LOADS):
                sp.dma_start(R[:, t:t + k, :], R_dram[:, t:t + k, :]).then_inc(s_load[n], 16)
                if n in E_AFTER:
                    a = E_AFTER.index(n)
                    sp.dma_start(E[:, EG * a:EG * a + EG, :], E_dram[:, EG * a:EG * a + EG, :]).then_inc(s_E[a], 16)
            sp.dma_start(FT[:, :], item_feat_T).then_inc(s_feat, 16)
            sp.dma_start(ET[:, :, :], user_emb_T.rearrange("p (q n) -> p q n", q=UNITS)).then_inc(s_ET, 16)
            sp.wait_ge(s_duT, 1)
            sp.dma_start(du_dram, duT[:, :]).then_inc(s_du_out, 16)
            sp.wait_ge(s_du_out, 16)
            by_half = du_dram.rearrange("(h q j) p -> h q (j p)", q=UNITS, h=2)
            sp.dma_start(DU[:, 0:1, :],
                         by_half[:, 0:1].unsqueeze(1).to_broadcast([2, H, 1, UW])).then_inc(s_DU0, 16)
            sp.dma_start(DU[:, 1:UNITS, :],
                         by_half[:, 1:UNITS].unsqueeze(1).to_broadcast([2, H, UNITS - 1, UW])).then_inc(s_DU, 16)
            for n, t in enumerate(ORDER):
                for b in range(2):
                    sp.wait_ge(*moved(n, b))
                sp.dma_start(Y_dram[:, t, :], Y[:, t, :]).then_inc(s_stored, 16)
            sp.wait_ge(s_stored, 16 * TILES)

        def move_scores(engine, eng, copy, n):
            for b in range(2):
                if MOVERS[n][b] == engine:
                    eng.wait_ge(s_C, 2 * n + b + 1)
                    copy(Y[:, ORDER[n], b * HALF:(b + 1) * HALF],
                         PB[ROTATION[n % 3]][:, b, 0:HALF]).then_inc(s_Y[engine], 1)

        def item_rows(eng, ops, b):
            rows = slice(H * b, H * b + H)
            for d in range(2):
                if d == 1:
                    eng.wait_ge(s_diXT[b], 1)
                ops.tensor_tensor(diXT[H * d:H * d + H, b, :], XT[rows, :], DI[rows, b, :],
                                  ALU.mult).then_inc(s_diXT[b], 1)

        @block.scalar
        def _(act):
            for g, (t, k) in enumerate(LOADS):
                for c in range(CHUNKS):
                    act.wait_ge(s_T, CHUNKS * g + c + 1)
                    nc.scalar.activation(RT[:, c, t * P:(t + k) * P], PB[1 + c // 2][0:IC, c % 2, 0:k * P],
                                         ACT.Identity, accum_out=csum[:, c, g:g + 1]).then_inc(s_RT, 1)
            act.wait_ge(s_A, 1)
            nc.scalar.copy(AG[:, 1, :], PB[0][:, 1, 0:HALF]).then_inc(s_AG[1], 1)
            act.wait_ge(s_DI_mm, 1)
            nc.scalar.copy(DI[:, :, :], PB[3][:, :, 0:HALF]).then_inc(s_DI, 1)
            for b in range(2):
                act.wait_ge(s_vs, b + 1)
                nc.scalar.activation(Vh[:, b, 0:HALF], vs[:, b, :], ACT.Identity, bias=gb[:, :]).then_inc(s_vhi, 1)
            for n in range(TILES):
                move_scores("A", act, nc.scalar.copy, n)

        @block.gpsimd
        def _(pool):
            nc.gpsimd.memset(half_neg[:, :], -0.5).then_inc(s_exp, 1)
            nc.gpsimd.memset(WD[:, :], 0.0).then_inc(s_wd0, 1)
            pool.wait_ge(s_small, 16)
            pool.wait_ge(s_wd0, 1)
            for h in range(2):
                b = slice(H * h, H * h + H)
                nc.gpsimd.tensor_copy(WD[b, b], WW[b, b]).then_inc(s_wd, 1)
            pool.wait_ge(s_wd, 2)
            pool.wait_ge(s_exp, 1)
            for n, (t, k) in enumerate(LOADS):
                pool.wait_ge(s_rdeg, n + 1)
                if n >= 1:
                    pool.wait_ge(s_duE, n)
                d = du_column(t)
                nc.gpsimd.tensor_tensor(du[:, d:d + k], rdeg[:, t:t + k], half_neg[:, t:t + k],
                                        ALU.pow).then_inc(s_du, 1)
                pool.wait_ge(s_du, n + 1)
                if t % EG == 0:
                    pool.wait_ge(s_E[t // EG], 16)
                nc.gpsimd.tensor_tensor(duE[:, t:t + k, :], E[:, t:t + k, :],
                                        du[:, d:d + k].unsqueeze(2).to_broadcast([P, k, H]),
                                        ALU.mult).then_inc(s_duE, 1)
            pool.wait_ge(s_duE, NL)
            pool.wait_ge(s_cdeg, 2)
            nc.gpsimd.tensor_tensor(di[:, :], cdeg1[:, :], half_neg[0:IC, 0:CHUNKS], ALU.pow).then_inc(s_di, 1)
            pool.wait_ge(s_di, 1)
            pool.wait_ge(s_x, 1)
            pool.wait_ge(s_DI, 1)
            item_rows(pool, nc.gpsimd, 1)
            pool.wait_ge(s_diXT[1], 2)
            pool.wait_ge(s_ET, 16)
            pool.wait_ge(s_DU0, 16)
            for q in range(UNITS):
                if q == 1:
                    pool.wait_ge(s_DU, 16)
                if q >= 1:
                    pool.wait_ge(s_duET, q)
                nc.gpsimd.tensor_tensor(duET[:, q, :], ET[:, q, :], DU[:, q, :], ALU.mult).then_inc(s_duET, 1)
            pool.wait_ge(s_duET, UNITS)
            for p, (q, u, w) in enumerate(PARTS):
                pool.wait_ge(s_us, p + 1)
                if p >= 1:
                    pool.wait_ge(s_ulo[1], p)
                bias = gb[H:2 * H, :].to_broadcast([H, w])
                nc.gpsimd.tensor_tensor(ub[H:2 * H, 0:w], us[H:2 * H, q % 2, u:u + w], bias, ALU.add).then_inc(s_ub, 1)
                pool.wait_ge(s_ub, p + 1)
                nc.gpsimd.tensor_tensor(UO[H:2 * H, q, 1, u:u + w], us[H:2 * H, q % 2, u:u + w], bias,
                                        ALU.add).then_inc(s_uhi[1], 1)
                pool.wait_ge(s_uhi[1], p + 1)
                nc.gpsimd.tensor_tensor(UO[0:H, q, 1, u:u + w], ub[H:2 * H, 0:w],
                                        UO[H:2 * H, q, 1, u:u + w].bitcast(f32), ALU.subtract).then_inc(s_ulo[1], 1)

        @block.vector
        def _(dve):
            nc.vector.memset(zeros[:, :], 0.0).then_inc(s_zeros, 1)
            nc.vector.memset(Vh[:, :, HALF:HPAD].bitcast(f32), 0.0).then_inc(s_pads, 1)
            nc.vector.memset(Vl[:, :, HALF:HPAD].bitcast(f32), 0.0).then_inc(s_pads, 1)

            def degrees(n):
                t, k = LOADS[n]
                dve.wait_ge(s_load[n], 16)
                nc.vector.reduce_sum(rsum[:, t:t + k], R[:, t:t + k, :], AX.X).then_inc(s_rsum, 1)
                dve.wait_ge(s_rsum, n + 1)
                nc.vector.tensor_scalar(rdeg[:, t:t + k], rsum[:, t:t + k], 1.0, FLOOR,
                                        ALU.add, ALU.max).then_inc(s_rdeg, 1)

            degrees(0)
            dve.wait_ge(s_fw_mm, 1)
            nc.vector.tensor_copy(FW[:, :], PB[0][:, 0, 0:H + 1]).then_inc(s_fw, 1)
            for n in range(1, NL):
                degrees(n)
            dve.wait_ge(s_duT_mm, 1)
            nc.vector.tensor_copy(duT[:, :], PB[1][0:TILES, 0, 0:P]).then_inc(s_duT, 1)

            dve.wait_ge(s_RT, NL * CHUNKS)
            nc.vector.reduce_sum(cdeg[:, :], csum[:, :, :], AX.X).then_inc(s_cdeg, 1)
            dve.wait_ge(s_cdeg, 1)
            nc.vector.tensor_scalar(cdeg1[:, :], cdeg[:, :], 1.0, FLOOR, ALU.add, ALU.max).then_inc(s_cdeg, 1)
            dve.wait_ge(s_fw, 1)
            dve.wait_ge(s_x_mm, 1)
            nc.vector.tensor_scalar(XT[:, :], PB[2][:, 1, 0:HALF], FW[:, H:H + 1], None, ALU.add).then_inc(s_x, 1)
            dve.wait_ge(s_A, 1)
            nc.vector.tensor_copy(AG[:, 0, :], PB[0][:, 0, 0:HALF]).then_inc(s_AG[0], 1)
            dve.wait_ge(s_di, 1)
            dve.wait_ge(s_xt, 1)
            nc.vector.tensor_tensor(diX[:, :, :].rearrange("p (b c) h -> p c b h", b=2),
                                    PB[1][0:IC, 1, 0:CHUNKS * H].rearrange("p (c b h) -> p c b h", b=2, h=H),
                                    di[:, :].rearrange("p (b c) -> p c b", b=2).unsqueeze(3)
                                    .to_broadcast([IC, CHUNKS // 2, 2, H]), ALU.mult).then_inc(s_diX, 1)

            def user_scaled(p):
                q, u, w = PARTS[p]
                dve.wait_ge(s_B, p + 1)
                if q == 0:
                    dve.wait_ge(s_DU0, 16)
                if q == 1:
                    dve.wait_ge(s_DU, 16)
                if q >= 2:
                    dve.wait_ge(s_uhi[1], q - 1)
                at = UW * (q // 2) + u
                nc.vector.tensor_tensor(us[:, q % 2, u:u + w], PB[1][:, q % 2, at:at + w],
                                        DU[:, q, u:u + w], ALU.mult).then_inc(s_us, 1)

            def user_parts(p):
                q, u, w = PARTS[p]
                dve.wait_ge(s_us, p + 1)
                nc.vector.tensor_scalar(UO[0:H, q, 0, u:u + w], us[0:H, q % 2, u:u + w], gb[0:H, :], None,
                                        ALU.add).then_inc(s_uhi[0], 1)
                dve.wait_ge(s_uhi[0], p + 1)
                nc.vector.scalar_tensor_tensor(out=UO[H:2 * H, q, 0, u:u + w], in0=us[0:H, q % 2, u:u + w],
                                               scalar=gb[0:H, :], in1=UO[0:H, q, 0, u:u + w].bitcast(f32),
                                               op0=ALU.add, op1=ALU.subtract).then_inc(s_ulo[0], 1)

            def item_low(b):
                dve.wait_ge(s_vhi, b + 1)
                nc.vector.scalar_tensor_tensor(out=Vl[:, b, 0:HALF], in0=vs[:, b, :], scalar=gb[:, :],
                                               in1=Vh[:, b, 0:HALF].bitcast(f32),
                                               op0=ALU.add, op1=ALU.subtract).then_inc(s_vlo, 1)

            dve.wait_ge(s_small, 16)
            dve.wait_ge(s_DI, 1)
            dve.wait_ge(s_x, 1)
            item_rows(dve, nc.vector, 0)
            for b in range(2):
                dve.wait_ge(s_V, b + 1)
                dve.wait_ge(s_diXT[b], 2)
                nc.vector.tensor_tensor(vd[:, b, :], PB[2][:, b, 0:HALF], diXT[:, b, :], ALU.add).then_inc(s_vd, 1)
                dve.wait_ge(s_vd, b + 1)
                nc.vector.tensor_tensor(vs[:, b, :], vd[:, b, :], DI[:, b, :], ALU.mult).then_inc(s_vs, 1)
            for b in range(2):
                item_low(b)
            for n in range(TILES):
                for p in range(len(PARTS)):
                    if BEFORE[p] == n:
                        user_scaled(p)
                        user_parts(p)
                move_scores("V", dve, nc.vector.tensor_copy, n)

        @block.tensor
        def _(pe):
            def transposes(g):
                t, k = LOADS[g]
                pe.wait_ge(s_load[g], 16)
                for c in range(CHUNKS):
                    if g >= 1:
                        pe.wait_ge(s_RT, CHUNKS * (g - 1) + c + 1)
                    for j in range(k):
                        last = nc.tensor.transpose(PB[1 + c // 2][0:IC, c % 2, j * P:(j + 1) * P],
                                                   R[:, t + j, c * IC:(c + 1) * IC], ident)
                    last.then_inc(s_T, 1)

            def aggregate(t):
                pe.wait_ge(s_duE, load_of(t + 1) + 1)
                if t == 0:
                    pe.wait_ge(s_fw, 1)
                for b in range(2):
                    for h in range(2):
                        last = nc.tensor.matmul(PB[0][H * h:H * h + H, b, 0:HALF], duE[:, t + h, :],
                                                R[:, t + h, b * HALF:(b + 1) * HALF],
                                                start=(t == 0), stop=(t == TILES - 2))
                if t == TILES - 2:
                    last.then_inc(s_A, 1)

            def propagate(p):
                q, u, w = PARTS[p]
                at = UW * (q // 2) + u
                out = PB[1][:, q % 2, at:at + w]
                if q >= 2:
                    pe.wait_ge(s_us, p if u else q - 1)
                for c in range(CHUNKS):
                    for h in range(2):
                        u0 = (2 * q + h) * UW + u
                        nc.tensor.matmul(out[H * h:H * h + H, :], diX[:, c, :], RT[:, c, u0:u0 + w],
                                         start=(c == 0), stop=False, skip_group_check=True)
                pe.wait_ge(s_duET, q + 1)
                nc.tensor.matmul(out, WD[:, :], duET[:, q, u:u + w], start=False, stop=True,
                                 skip_group_check=True).then_inc(s_B, 1)

            def score(n):
                t = ORDER[n]
                q, h, j = t // 4, t // 2 % 2, t % 2
                pe.wait_ge(s_ulo[h], part_of(t) + 1)
                if n == 0:
                    pe.wait_ge(s_DI, 1)
                if n == 1:
                    for b in range(2):
                        pe.wait_ge(s_AG[b], 1)
                if n == 2:
                    pe.wait_ge(s_vd, 2)
                for b in range(2):
                    if n >= 3:
                        pe.wait_ge(*moved(n - 3, b))
                    for V in (Vh, Vl):
                        if n == 0:
                            pe.wait_ge(s_vhi if V is Vh else s_vlo, b + 1)
                        last = nc.tensor.matmul(PB[ROTATION[n % 3]][:, b, 0:HPAD], UO[:, q, h, j * P:(j + 1) * P],
                                                V[:, b, :], start=(V is Vh), stop=(V is Vl))
                    last.then_inc(s_C, 1)

            def features():
                pe.wait_ge(s_feat, 16)
                pe.wait_ge(s_fw, 1)
                pe.wait_ge(s_RT, CHUNKS * NL)
                for b in range(2):
                    last = nc.tensor.matmul(PB[2][H * b:H * b + H, 1, 0:HALF], FW[:, 0:H],
                                            FT[:, b * HALF:(b + 1) * HALF], start=True, stop=True)
                last.then_inc(s_x_mm, 1)

            def warm(columns):
                nc.tensor.matmul(PB[1][:, 0, 0:columns], zeros[:, :].to_broadcast([P, P]),
                                 zeros[:, :].to_broadcast([P, columns]), start=True, stop=True)

            pe.wait_ge(s_zeros, 1)
            for _ in range(5):
                warm(4 * P)
            pe.wait_ge(s_small, 16)
            nc.tensor.matmul(PB[0][:, 0, 0:H], fwT, WW[0:H, 0:H], start=True, stop=True)
            nc.tensor.matmul(PB[0][:, 0, H:H + 1], WW[0:H, :], fb, start=True, stop=True).then_inc(s_fw_mm, 1)
            for _ in range(2):
                warm(P)
            transposes(0)
            transposes(1)
            transposes(2)
            aggregate(0)
            transposes(3)
            transposes(4)
            aggregate(2)
            transposes(5)
            aggregate(4)
            transposes(6)
            aggregate(6)
            transposes(7)
            transposes(8)
            aggregate(8)
            transposes(9)
            aggregate(10)
            pe.wait_ge(s_du, NL)
            pe.wait_ge(s_RT, CHUNKS * (NL - 1) + 1)
            nc.tensor.transpose(PB[1][0:TILES, 0, 0:P], du[:, :], ident).then_inc(s_duT_mm, 1)
            aggregate(12)
            features()
            aggregate(14)
            pe.wait_ge(s_x, 1)
            for c in range(CHUNKS // 2):
                last = nc.tensor.transpose(PB[1][0:IC, 1, c * P:(c + 1) * P], XT[:, c * IC:(c + 1) * IC], ident)
            last.then_inc(s_xt, 1)
            pe.wait_ge(s_RT, CHUNKS * NL)
            pe.wait_ge(s_di, 1)
            for c in range(CHUNKS):
                at = IC * (c % 3)
                last = nc.tensor.transpose(PB[3][:, c // 3, at:at + IC], di[:, c:c + 1].to_broadcast([IC, P]),
                                           ident[0:IC, 0:IC])
            last.then_inc(s_DI_mm, 1)
            pe.wait_ge(s_duT, 1)
            pe.wait_ge(s_wd, 2)
            for b in range(2):
                pe.wait_ge(s_AG[b], 1)
                nc.tensor.matmul(PB[2][:, b, 0:HALF], WW[:, :], AG[:, b, :], start=True, stop=True).then_inc(s_V, 1)
            pe.wait_ge(s_diX, 1)
            pe.wait_ge(s_pads, 2)
            for n in range(TILES):
                for p in range(len(PARTS)):
                    if BEFORE[p] == n:
                        propagate(p)
                score(n)


def kernel(r_user_item_matrix, r_user_emb, L0_rec_item_feature_matrix, L0_rec_feat_w, L0_rec_feat_b,
           L0_rec_gcn_w, L0_rec_gcn_b):
    import numpy as np
    import concourse.bacc as bacc
    from concourse.bass_utils import run_bass_kernel_spmd

    ratings, emb, feats, feat_w, feat_b, gcn_w, gcn_b = (
        np.asarray(a) for a in (r_user_item_matrix, r_user_emb, L0_rec_item_feature_matrix, L0_rec_feat_w,
                                L0_rec_feat_b, L0_rec_gcn_w, L0_rec_gcn_b))
    users, items = ratings.shape
    hidden = emb.shape[1]
    emb_T = emb.reshape(128, 4, 2, 2, hidden).transpose(2, 4, 1, 3, 0).reshape(2 * hidden, users // 2)
    small = np.zeros((128, 3 * 128 + 2), dtype=ratings.dtype)
    small[:, 0:128] = np.eye(128)
    small[:, 128:256] = np.tile(gcn_w, (2, 2))
    small[0:hidden, 256:384] = feat_w.T
    small[:, 384] = np.tile(gcn_b, 2)
    small[0:hidden, 385] = feat_b
    arrays = {"ratings": ratings, "user_emb": emb, "user_emb_T": emb_T, "item_feat_T": feats.T, "small": small}
    arrays = {name: np.ascontiguousarray(a) for name, a in arrays.items()}
    nc = bacc.Bacc("TRN2", target_bir_lowering=False, num_devices=1)
    args = [nc.dram_tensor(name, a.shape, mybir.dt.from_np(a.dtype), kind="ExternalInput").ap()
            for name, a in arrays.items()]
    out = nc.dram_tensor("scores", (users, items), mybir.dt.float32, kind="ExternalOutput").ap()
    lightgcn_scores(nc, *args, out)
    result = run_bass_kernel_spmd(nc, [arrays], core_ids=[0])
    return result.results[0]["scores"]
```
